# Optimizing a Trainium2 kernel written in Bass

```python
import numpy as np
import jax
import jax.numpy as jnp

def _softmax(x, axis=-1):
    return jax.nn.softmax(x, axis=axis)

def _gelu(x):
    return jax.nn.gelu(x, approximate=True)

def _silu(x):
    return jax.nn.silu(x)

def _sigmoid(x):
    return jax.nn.sigmoid(x)

def _layernorm(x, axis=-1, eps=1e-05):
    m = jnp.mean(x, axis=axis, keepdims=True)
    v = jnp.var(x, axis=axis, keepdims=True)
    return (x - m) / jnp.sqrt(v + eps)

def _scatter_add(tgt, idx, src, axis=0):
    return tgt.at[idx].add(src)

def _segment_sum(src, seg, n):
    return jax.ops.segment_sum(src, seg, n)
kernel_name = 'mk_dlrm_tower_d1_rec_r8_28e3a6'

def setup_inputs(seed: int=0):
    np.random.seed(seed)
    _w = jnp.asarray

    def _rec_inputs():
        import jax
        import jax.numpy as jnp
        _tk = jax.random.key(seed)
        dense_ctx = jax.random.normal(jax.random.fold_in(_tk, 190), (2048, 16), jnp.float32)
        ids = jnp.stack([jax.random.randint(jax.random.fold_in(_tk, 200 + f), (2048,), 0, v, jnp.int32) for f, v in enumerate([12500, 1250, 1000, 125000, 1250, 1250, 12500, 1000, 1000, 1000, 1250, 1250, 12500, 1000, 1250, 1250, 1250, 1250, 12500, 12500, 1250, 12500, 1250, 1250, 1250, 1250, 1000])], axis=1)
        tbl_0 = 0.05 * jax.random.normal(jax.random.fold_in(_tk, 500 + 0), (12500, 128), jnp.float32)
        tbl_1 = 0.05 * jax.random.normal(jax.random.fold_in(_tk, 500 + 1), (1250, 128), jnp.float32)
        tbl_2 = 0.05 * jax.random.normal(jax.random.fold_in(_tk, 500 + 2), (1000, 128), jnp.float32)
        tbl_3 = 0.05 * jax.random.normal(jax.random.fold_in(_tk, 500 + 3), (125000, 128), jnp.float32)
        tbl_4 = 0.05 * jax.random.normal(jax.random.fold_in(_tk, 500 + 4), (1250, 128), jnp.float32)
        tbl_5 = 0.05 * jax.random.normal(jax.random.fold_in(_tk, 500 + 5), (1250, 128), jnp.float32)
        tbl_6 = 0.05 * jax.random.normal(jax.random.fold_in(_tk, 500 + 6), (12500, 128), jnp.float32)
        tbl_7 = 0.05 * jax.random.normal(jax.random.fold_in(_tk, 500 + 7), (1000, 128), jnp.float32)
        tbl_8 = 0.05 * jax.random.normal(jax.random.fold_in(_tk, 500 + 8), (1000, 128), jnp.float32)
        tbl_9 = 0.05 * jax.random.normal(jax.random.fold_in(_tk, 500 + 9), (1000, 128), jnp.float32)
        tbl_10 = 0.05 * jax.random.normal(jax.random.fold_in(_tk, 500 + 10), (1250, 128), jnp.float32)
        tbl_11 = 0.05 * jax.random.normal(jax.random.fold_in(_tk, 500 + 11), (1250, 128), jnp.float32)
        tbl_12 = 0.05 * jax.random.normal(jax.random.fold_in(_tk, 500 + 12), (12500, 128), jnp.float32)
        tbl_13 = 0.05 * jax.random.normal(jax.random.fold_in(_tk, 500 + 13), (1000, 128), jnp.float32)
        tbl_14 = 0.05 * jax.random.normal(jax.random.fold_in(_tk, 500 + 14), (1250, 128), jnp.float32)
        tbl_15 = 0.05 * jax.random.normal(jax.random.fold_in(_tk, 500 + 15), (1250, 128), jnp.float32)
        tbl_16 = 0.05 * jax.random.normal(jax.random.fold_in(_tk, 500 + 16), (1250, 128), jnp.float32)
        tbl_17 = 0.05 * jax.random.normal(jax.random.fold_in(_tk, 500 + 17), (1250, 128), jnp.float32)
        tbl_18 = 0.05 * jax.random.normal(jax.random.fold_in(_tk, 500 + 18), (12500, 128), jnp.float32)
        tbl_19 = 0.05 * jax.random.normal(jax.random.fold_in(_tk, 500 + 19), (12500, 128), jnp.float32)
        tbl_20 = 0.05 * jax.random.normal(jax.random.fold_in(_tk, 500 + 20), (1250, 128), jnp.float32)
        tbl_21 = 0.05 * jax.random.normal(jax.random.fold_in(_tk, 500 + 21), (12500, 128), jnp.float32)
        tbl_22 = 0.05 * jax.random.normal(jax.random.fold_in(_tk, 500 + 22), (1250, 128), jnp.float32)
        tbl_23 = 0.05 * jax.random.normal(jax.random.fold_in(_tk, 500 + 23), (1250, 128), jnp.float32)
        tbl_24 = 0.05 * jax.random.normal(jax.random.fold_in(_tk, 500 + 24), (1250, 128), jnp.float32)
        tbl_25 = 0.05 * jax.random.normal(jax.random.fold_in(_tk, 500 + 25), (1250, 128), jnp.float32)
        tbl_26 = 0.05 * jax.random.normal(jax.random.fold_in(_tk, 500 + 26), (1000, 128), jnp.float32)
        _rk = jax.random.fold_in(_tk, 7)
        W_top1 = 0.0161733 * jax.random.normal(jax.random.fold_in(_tk, 801), (3823, 512), jnp.float32)
        W_top2 = 0.0441942 * jax.random.normal(jax.random.fold_in(_tk, 802), (512, 256), jnp.float32)
        W_top3 = 0.0625 * jax.random.normal(jax.random.fold_in(_tk, 803), (256, 1), jnp.float32)
        b_top1 = jnp.zeros((512,), jnp.float32)
        b_top2 = jnp.zeros((256,), jnp.float32)
        return (dense_ctx, ids, tbl_0, tbl_1, tbl_2, tbl_3, tbl_4, tbl_5, tbl_6, tbl_7, tbl_8, tbl_9, tbl_10, tbl_11, tbl_12, tbl_13, tbl_14, tbl_15, tbl_16, tbl_17, tbl_18, tbl_19, tbl_20, tbl_21, tbl_22, tbl_23, tbl_24, tbl_25, tbl_26, W_top1, b_top1, W_top2, b_top2, W_top3)
    dense_ctx, ids, tbl_0, tbl_1, tbl_2, tbl_3, tbl_4, tbl_5, tbl_6, tbl_7, tbl_8, tbl_9, tbl_10, tbl_11, tbl_12, tbl_13, tbl_14, tbl_15, tbl_16, tbl_17, tbl_18, tbl_19, tbl_20, tbl_21, tbl_22, tbl_23, tbl_24, tbl_25, tbl_26, W_top1, b_top1, W_top2, b_top2, W_top3 = _rec_inputs()

    def _L0_rec_setup():
        import jax, jax.numpy as jnp
        import numpy as np
        NUM_FEATURES = 27
        FEATURE_DIM = 128
        BATCH = 2048
        _TRIU_I, _TRIU_J = np.triu_indices(NUM_FEATURES, k=1)
        key = jax.random.key(seed)
        embeddings = jax.random.normal(key, (BATCH, NUM_FEATURES, FEATURE_DIM), dtype=jnp.float32)
        return {'embeddings': embeddings}
    _L0_rec_all = _L0_rec_setup()
    _L0_rec_in = {k: v for k, v in _L0_rec_all.items() if k in ()}
    del _L0_rec_all
    return {'dense_ctx': dense_ctx, 'ids': ids, 'tbl_0': tbl_0, 'tbl_1': tbl_1, 'tbl_2': tbl_2, 'tbl_3': tbl_3, 'tbl_4': tbl_4, 'tbl_5': tbl_5, 'tbl_6': tbl_6, 'tbl_7': tbl_7, 'tbl_8': tbl_8, 'tbl_9': tbl_9, 'tbl_10': tbl_10, 'tbl_11': tbl_11, 'tbl_12': tbl_12, 'tbl_13': tbl_13, 'tbl_14': tbl_14, 'tbl_15': tbl_15, 'tbl_16': tbl_16, 'tbl_17': tbl_17, 'tbl_18': tbl_18, 'tbl_19': tbl_19, 'tbl_20': tbl_20, 'tbl_21': tbl_21, 'tbl_22': tbl_22, 'tbl_23': tbl_23, 'tbl_24': tbl_24, 'tbl_25': tbl_25, 'tbl_26': tbl_26, 'W_top1': W_top1, 'b_top1': b_top1, 'W_top2': W_top2, 'b_top2': b_top2, 'W_top3': W_top3}

def reference(dense_ctx, ids, tbl_0, tbl_1, tbl_2, tbl_3, tbl_4, tbl_5, tbl_6, tbl_7, tbl_8, tbl_9, tbl_10, tbl_11, tbl_12, tbl_13, tbl_14, tbl_15, tbl_16, tbl_17, tbl_18, tbl_19, tbl_20, tbl_21, tbl_22, tbl_23, tbl_24, tbl_25, tbl_26, W_top1, b_top1, W_top2, b_top2, W_top3):
    import jax
    import jax.numpy as jnp

    def _L0_rec_ref(embeddings):
        import jax, jax.numpy as jnp
        import numpy as np
        NUM_FEATURES = 27
        FEATURE_DIM = 128
        BATCH = 2048
        _TRIU_I, _TRIU_J = np.triu_indices(NUM_FEATURES, k=1)
        B = embeddings.shape[0]
        interactions = jnp.einsum('bfd,bgd->bfg', embeddings, embeddings)
        flat_interactions = interactions[:, _TRIU_I, _TRIU_J]
        flat_embeddings = embeddings.reshape(B, -1)
        return jnp.concatenate([flat_embeddings, flat_interactions], axis=1)
    e = jnp.stack([tbl_0[ids[:, 0]], tbl_1[ids[:, 1]], tbl_2[ids[:, 2]], tbl_3[ids[:, 3]], tbl_4[ids[:, 4]], tbl_5[ids[:, 5]], tbl_6[ids[:, 6]], tbl_7[ids[:, 7]], tbl_8[ids[:, 8]], tbl_9[ids[:, 9]], tbl_10[ids[:, 10]], tbl_11[ids[:, 11]], tbl_12[ids[:, 12]], tbl_13[ids[:, 13]], tbl_14[ids[:, 14]], tbl_15[ids[:, 15]], tbl_16[ids[:, 16]], tbl_17[ids[:, 17]], tbl_18[ids[:, 18]], tbl_19[ids[:, 19]], tbl_20[ids[:, 20]], tbl_21[ids[:, 21]], tbl_22[ids[:, 22]], tbl_23[ids[:, 23]], tbl_24[ids[:, 24]], tbl_25[ids[:, 25]], tbl_26[ids[:, 26]]], axis=1)
    z = _L0_rec_ref(e)
    z = z.reshape(z.shape[0], -1)
    h = jnp.concatenate([z, dense_ctx], axis=1)
    h = jnp.maximum(h @ W_top1 + b_top1, 0.0)
    h = jnp.maximum(h @ W_top2 + b_top2, 0.0)
    y = h @ W_top3
    return y

_drawn_inputs = setup_inputs


def setup_inputs(seed=0):
    import zlib

    import numpy as np

    out = dict(_drawn_inputs(seed))
    spreads = {'b_top1': (0.0, 0.1), 'b_top2': (0.0, 0.1)}
    factors = {}
    for name, (base, spread) in spreads.items():
        noise = np.random.default_rng([zlib.crc32(name.encode()), seed]).standard_normal(out[name].shape)
        drawn = base * np.exp(spread * noise) if base else spread * noise
        out[name] = jnp.asarray(drawn.astype(out[name].dtype))
    for name, factor in factors.items():
        out[name] = (out[name] * factor).astype(out[name].dtype)
    return out
```

```python
from contextlib import ExitStack

import numpy as np

import concourse.bass as bass
from concourse import mybir

F32 = mybir.dt.float32
F32R = mybir.dt.float32r
I32 = mybir.dt.int32
ALU = mybir.AluOpType
ACT = mybir.ActivationFunctionType

P = 128
FEATURES = 27
DIM = 128
BATCH = 2048
DENSE = 16
H1 = 512
H2 = 256
TILES = BATCH // P
CHUNK = 4
CHUNKS = [list(range(f, min(f + CHUNK, FEATURES))) for f in range(0, FEATURES, CHUNK)]
NQ = len(CHUNKS)
HIDDEN_BLOCKS = H1 // P

DIST = (FEATURES - 1) // 2
RUNS = FEATURES - 1
PAIRS = FEATURES * (FEATURES - 1) // 2
HALF = PAIRS - DIST * RUNS
DENSE_AT = PAIRS
ONE_AT = DENSE_AT + DENSE
EXTRA_BLOCKS = -(-(ONE_AT + 1) // P)
EXTRAS = EXTRA_BLOCKS * P
K_BLOCKS = FEATURES + EXTRA_BLOCKS
W_PAIRS = K_BLOCKS // 2
W_SLOTS = 3
BLOCK32 = 32


def extra_rows():
    flat = [(FEATURES + 1) * f + k for f in range(RUNS) for k in range(1, DIST + 1)]
    flat += [(FEATURES + 1) * f + DIST + 1 for f in range(HALF)]
    rows = []
    for v in flat:
        i, j = sorted(divmod(v, FEATURES))
        rows.append(FEATURES * DIM + i * FEATURES - i * (i + 1) // 2 + j - i - 1)
    assert sorted(rows) == list(range(FEATURES * DIM, FEATURES * DIM + PAIRS))
    return rows


class Tile:

    def __init__(self, t, half, parity):
        self.t, self.half, self.parity = t, half, parity

    def chunks(self, q):
        return self.t * NQ + (q + 1)

    def bank(self, q):
        return (self.parity * NQ + q) % 2


def tile_of(t):
    return Tile(t, t // 2, t % 2)


def over_tiles(engine, body):
    body(tile_of(0), None, 0)
    body(tile_of(1), tile_of(0), 1)
    with engine.Fori(1, TILES // 2) as i:
        even = Tile(i * 2, i, 0)
        odd = Tile(i * 2 + 1, i, 1)
        body(even, Tile(i * 2 - 1, i - 1, 1), 2)
        body(odd, even, 3)
    body(None, tile_of(TILES - 1), TILES)


def build(nc, ids, dense, tables, w_embed, w_extra, w2, b2, w3, out):
    with ExitStack() as ctx:
        def sb(name, shape, dt=F32):
            return ctx.enter_context(nc.sbuf_tensor(name, shape, dt))

        def pb(name):
            return ctx.enter_context(nc.psum_tensor(name, [P, 512], F32))

        def sem(name):
            return ctx.enter_context(nc.semaphore(name))

        w_hi = sb("w_hi", [P, K_BLOCKS, H1], F32R)
        w_lo = sb("w_lo", [P, K_BLOCKS, H1], F32R)
        w2_sb = sb("w2_sb", [P, HIDDEN_BLOCKS, H2])
        b2_sb = sb("b2_sb", [P, H2])
        w3_sb = sb("w3_sb", [P, H2])
        ident = sb("ident", [P, P])
        ids_sb = [sb(f"ids{b}", [P, FEATURES], I32) for b in range(2)]
        rows = sb("rows", [P, FEATURES, DIM])
        embT = [sb(f"embT{b}", [P, P * FEATURES]) for b in range(2)]
        embT_v = [e[:, :].rearrange("d (s f) -> d s f", f=FEATURES) for e in embT]
        emb_hi = [sb(f"emb_hi{b}", [P, CHUNK * P], F32R) for b in range(2)]
        emb_lo = [sb(f"emb_lo{b}", [P, CHUNK * P], F32R) for b in range(2)]
        w_raw = embT[1][:, 0:W_SLOTS * 2 * H1].rearrange("p (s k n) -> p s k n", s=W_SLOTS, k=2)
        prod32 = sb("prod32", [P, FEATURES, BLOCK32])
        prod = sb("prod", [P, FEATURES * FEATURES])
        extra = [sb(f"extra{b}", [P, EXTRAS]) for b in range(2)]
        extra_hi = sb("extra_hi", [P, EXTRAS], F32R)
        extra_lo = sb("extra_lo", [P, EXTRAS], F32R)
        h1 = sb("h1", [P, H1])
        h1T = sb("h1T", [P, H1])
        h2 = sb("h2", [P, H2])
        h2w = sb("h2w", [P, H2])
        y = [sb(f"y{b}", [P, 1]) for b in range(2)]

        acc = [pb(f"acc{b}") for b in range(2)]
        trans = [pb(f"trans{b}") for b in range(2)]
        gram = ctx.enter_context(nc.psum_tensor("gram", [P, BLOCK32, BLOCK32], F32))
        misc = pb("misc")
        second = pb("second")

        w_loaded = [sem(f"w_loaded{s}") for s in range(W_SLOTS)]
        small_loaded = sem("small_loaded")
        ids_loaded = [sem(f"ids_loaded{b}") for b in range(2)]
        dense_loaded = [sem(f"dense_loaded{b}") for b in range(2)]
        gathered = [sem(f"gathered{q}") for q in range(NQ)]
        stored = [sem(f"stored{b}") for b in range(2)]
        ident_zero = sem("ident_zero")
        ident_ready = sem("ident_ready")
        cleared = sem("cleared")
        w_hi_ready = sem("w_hi_ready")
        w_lo_ready = sem("w_lo_ready")
        rows_free = sem("rows_free")
        transposed = sem("transposed")
        hi_ready = sem("hi_ready")
        lo_ready = sem("lo_ready")
        raw_ready = sem("raw_ready")
        multiplied = sem("multiplied")
        gram_ready = sem("gram_ready")
        prod32_ready = sem("prod32_ready")
        prod_ready = sem("prod_ready")
        extra_ready = sem("extra_ready")
        extra_transposed = sem("extra_transposed")
        extra_hi_ready = sem("extra_hi_ready")
        extra_lo_ready = sem("extra_lo_ready")
        acc_ready = sem("acc_ready")
        h1_ready = sem("h1_ready")
        h1_transposed = sem("h1_transposed")
        h1T_ready = sem("h1T_ready")
        second_ready = sem("second_ready")
        h2_ready = sem("h2_ready")
        y_ready = sem("y_ready")

        block = ctx.enter_context(nc.Block())

        @block.sync
        def _(sp):
            def load_ids(t, row, parity):
                sp.dma_start(ids_sb[parity][:, :], ids[row, :]).then_inc(ids_loaded[parity], 16)

            load_ids(0, bass.ds(0, P), 0)
            load_ids(1, bass.ds(P, P), 1)
            for j in range(W_PAIRS):
                if j >= W_SLOTS:
                    sp.wait_ge(w_lo_ready, j - W_SLOTS + 1)
                k = 2 * j
                for half in range(2):
                    src = w_embed[k + half] if k + half < FEATURES else w_extra[k + half - FEATURES]
                    sp.dma_start(w_raw[:, j % W_SLOTS, half, :], src).then_inc(w_loaded[j % W_SLOTS], 16)
                if j == 1:
                    sp.dma_start(w2_sb[:, :, :], w2.rearrange("(k p) n -> p k n", p=P)).then_inc(small_loaded, 16)
                    sp.dma_start(b2_sb[:, :], b2.partition_broadcast(P)).then_inc(small_loaded, 16)
                    sp.dma_start(w3_sb[:, :], w3.partition_broadcast(P)).then_inc(small_loaded, 16)

            def step(tile, prev, n):
                if tile is not None:
                    if n >= 2:
                        sp.wait_ge(transposed, tile.t * NQ - NQ)
                        load_ids(tile.t, bass.ds(tile.t * P, P), tile.parity)
                        sp.wait_ge(extra_transposed, tile.t - 1)
                    else:
                        sp.wait_ge(cleared, 3)
                    sp.dma_start(extra[tile.parity][:, DENSE_AT:ONE_AT],
                                 dense[bass.ds(tile.t * P, P), :]).then_inc(dense_loaded[tile.parity], 16)
                if prev is not None and n >= 2:
                    store(Tile(prev.t - 1, prev.half if prev.parity else prev.half - 1, 1 - prev.parity))

            def store(done):
                sp.wait_ge(y_ready, done.t + 1)
                sp.dma_start(out[bass.ds(done.t * P, P), :], y[done.parity][:, :]).then_inc(
                    stored[done.parity], 16)

            over_tiles(sp, step)
            store(tile_of(TILES - 1))
            for b in range(2):
                sp.wait_ge(stored[b], 16 * (TILES // 2))

        @block.gpsimd
        def _(pool):
            nc.gpsimd.memset(ident[:, :], 0.0).then_inc(ident_zero, 1)
            pool.wait_ge(ident_zero, 1)
            nc.gpsimd.affine_select(out=ident[:, :], in_=ident[:, :], compare_op=ALU.not_equal, fill=1.0,
                                    base=0, pattern=[[-1, P]], channel_multiplier=1).then_inc(ident_ready, 1)

            def step(tile, prev, n):
                if tile is None:
                    return
                pool.wait_ge(ids_loaded[tile.parity], tile.half * 16 + 16)
                for q, features in enumerate(CHUNKS):
                    if n >= 1:
                        pool.wait_ge(transposed, tile.chunks(q) - NQ)
                    pool.sem_inc(rows_free, 1)
                    for f in features:
                        nc.gpsimd.indirect_dma_start(
                            rows[:, f, :], None, tables[f],
                            bass.IndirectOffsetOnAxis(ap=ids_sb[tile.parity][:, f:f + 1], axis=0),
                        ).then_inc(gathered[q], 16)

            over_tiles(pool, step)

        @block.scalar
        def _(act):
            def split_weights(j):
                act.wait_ge(w_loaded[j % W_SLOTS], 32 * (j // W_SLOTS + 1))
                nc.scalar.copy(w_hi[:, 2 * j:2 * j + 2, :], w_raw[:, j % W_SLOTS]).then_inc(w_hi_ready, 1)

            def embedding_hi(tile, q, n):
                width = len(CHUNKS[q]) * P
                b = tile.bank(q)
                act.wait_ge(transposed, tile.chunks(q))
                if n >= 1 or q >= 2:
                    act.wait_ge(multiplied, tile.chunks(q) - 2)
                nc.scalar.copy(emb_hi[b][:, :width], trans[b][:, :width]).then_inc(hi_ready, 1)

            def compact_products(prev, n):
                act.wait_ge(prod32_ready, prev.t + 1)
                if n >= 2:
                    act.wait_ge(extra_ready, prev.t * 2)
                nc.scalar.copy(prod[:, :].rearrange("p (g f) -> p g f", f=FEATURES),
                               prod32[:, :, 0:FEATURES]).then_inc(prod_ready, 1)

            def extras_hi(prev, n):
                act.wait_ge(extra_transposed, prev.t + 1)
                if n >= 2:
                    act.wait_ge(acc_ready, prev.t)
                nc.scalar.copy(extra_hi[:, :], misc[:, :EXTRAS]).then_inc(extra_hi_ready, 1)

            def relu1(prev, n):
                act.wait_ge(acc_ready, prev.t + 1)
                if n >= 2:
                    act.wait_ge(h1_transposed, prev.t)
                nc.scalar.activation(h1[:, :], acc[prev.parity][:, :], ACT.Relu).then_inc(h1_ready, 1)

            def copy_h1T(prev, n):
                act.wait_ge(h1_transposed, prev.t + 1)
                if n >= 2:
                    act.wait_ge(second_ready, prev.t)
                nc.scalar.copy(h1T[:, :], misc[:, :]).then_inc(h1T_ready, 1)

            def step(tile, prev, n):
                later = {1: compact_products, 3: extras_hi, 4: relu1, 5: copy_h1T}
                for q in range(NQ):
                    if n == 0:
                        split_weights(2 * q)
                        split_weights(2 * q + 1)
                    if tile is not None:
                        embedding_hi(tile, q, n)
                    if prev is not None and q in later:
                        later[q](prev, n)
                if n == 0:
                    split_weights(W_PAIRS - 1)

            over_tiles(act, step)

        @block.vector
        def _(dve):
            nc.vector.memset(gram[:, :, :], 0.0).then_inc(cleared, 1)
            for b in range(2):
                nc.vector.memset(extra[b][:, ONE_AT:], 0.0).then_inc(cleared, 1)
            dve.wait_ge(cleared, 3)
            for b in range(2):
                nc.vector.memset(extra[b][:, ONE_AT:ONE_AT + 1], 1.0).then_inc(cleared, 1)

            def split_weights(j):
                dve.wait_ge(w_hi_ready, j + 1)
                nc.vector.tensor_tensor(w_lo[:, 2 * j:2 * j + 2, :], w_raw[:, j % W_SLOTS],
                                        w_hi[:, 2 * j:2 * j + 2, :].bitcast(F32), ALU.subtract).then_inc(w_lo_ready, 1)

            def embedding_lo(tile, q, n):
                count = len(CHUNKS[q])
                b = tile.bank(q)
                dve.wait_ge(hi_ready, tile.chunks(q))
                nc.vector.tensor_tensor(emb_lo[b][:, :count * P], trans[b][:, :count * P],
                                        emb_hi[b][:, :count * P].bitcast(F32), ALU.subtract).then_inc(lo_ready, 1)
                if q == 0 and n == 1:
                    dve.wait_ge(w_lo_ready, W_PAIRS)
                if q == 0 and n >= 2:
                    dve.wait_ge(gram_ready, tile.t - 1)
                f0 = CHUNKS[q][0]
                nc.vector.tensor_copy(
                    embT_v[tile.parity][:, :, f0:f0 + count],
                    trans[b][:, :count * P].rearrange("d (f s) -> d s f", f=count)).then_inc(raw_ready, 1)

            def products_by_sample(prev, n):
                dve.wait_ge(gram_ready, prev.t + 1)
                if n >= 2:
                    dve.wait_ge(prod_ready, prev.t)
                nc.vector.transpose(prod32[:, :, :],
                                    gram[:, :, 0:FEATURES].rearrange("p s g -> p g s")).then_inc(prod32_ready, 1)

            def extras(prev, n):
                dve.wait_ge(prod_ready, prev.t + 1)
                if n >= 3:
                    dve.wait_ge(extra_transposed, prev.t - 1)
                runs = prod[:, 0:RUNS * (FEATURES + 1)].rearrange("p (f k) -> p f k", k=FEATURES + 1)
                nc.vector.tensor_copy(extra[prev.parity][:, 0:RUNS * DIST].rearrange("p (f k) -> p f k", k=DIST),
                                      runs[:, :, 1:DIST + 1]).then_inc(extra_ready, 1)
                nc.vector.tensor_copy(extra[prev.parity][:, RUNS * DIST:PAIRS],
                                      runs[:, 0:HALF, DIST + 1]).then_inc(extra_ready, 1)

            def extras_lo(prev, n):
                dve.wait_ge(extra_hi_ready, prev.t + 1)
                nc.vector.tensor_tensor(extra_lo[:, :], misc[:, :EXTRAS], extra_hi[:, :].bitcast(F32),
                                        ALU.subtract).then_inc(extra_lo_ready, 1)

            def last_layers(prev, n):
                if n == 1:
                    dve.wait_ge(small_loaded, 48)
                dve.wait_ge(second_ready, prev.t + 1)
                if n >= 2:
                    dve.wait_ge(y_ready, prev.t)
                nc.vector.tensor_tensor(h2[:, :], second[:, :H2], b2_sb[:, :], ALU.add).then_inc(h2_ready, 1)
                dve.wait_ge(h2_ready, prev.t + 1)
                if n >= 3:
                    dve.wait_ge(stored[prev.parity], prev.half * 16)
                nc.vector.scalar_tensor_tensor(out=h2w[:, :], in0=h2[:, :], scalar=0.0, in1=w3_sb[:, :],
                                               op0=ALU.max, op1=ALU.mult,
                                               accum_out=y[prev.parity][:, :]).then_inc(y_ready, 1)

            def step(tile, prev, n):
                later = {1: products_by_sample, 2: extras, 3: extras_lo, 6: last_layers}
                for q in range(NQ):
                    if n == 0:
                        split_weights(2 * q)
                        split_weights(2 * q + 1)
                    if tile is not None:
                        embedding_lo(tile, q, n)
                    if prev is not None and q in later:
                        later[q](prev, n)
                if n == 0:
                    split_weights(W_PAIRS - 1)

            over_tiles(dve, step)

        @block.tensor
        def _(pe):
            pe.wait_ge(ident_ready, 1)

            def transpose_rows(tile, q, n):
                pe.wait_ge(gathered[q], tile.t * (16 * len(CHUNKS[q])) + 16 * len(CHUNKS[q]))
                if n >= 1 or q >= 2:
                    pe.wait_ge(raw_ready, tile.chunks(q) - 2)
                for a, f in enumerate(CHUNKS[q]):
                    last = nc.tensor.transpose(trans[tile.bank(q)][:, a * P:(a + 1) * P], rows[:, f, :], ident[:, :])
                last.then_inc(transposed, 1)

            def three_passes(into, hi, lo, k, first, final):
                nc.tensor.matmul(into, hi, w_hi[:, k, :], start=first, stop=False)
                nc.tensor.matmul(into, hi, w_lo[:, k, :], start=False, stop=False)
                return nc.tensor.matmul(into, lo, w_hi[:, k, :], start=False, stop=final)

            def multiply_rows(tile, q, n):
                if n == 0:
                    pe.wait_ge(w_lo_ready, 2 * q + 2)
                if q == 0 and n >= 2:
                    pe.wait_ge(h1_ready, tile.t - 1)
                pe.wait_ge(lo_ready, tile.chunks(q))
                for a, f in enumerate(CHUNKS[q]):
                    part = slice(a * P, (a + 1) * P)
                    last = three_passes(acc[tile.parity][:, :], emb_hi[tile.bank(q)][:, part],
                                        emb_lo[tile.bank(q)][:, part], f, f == 0, False)
                last.then_inc(multiplied, 1)

            def products(prev, n):
                pe.wait_ge(raw_ready, prev.t * NQ + NQ)
                if n == 1:
                    pe.wait_ge(cleared, 1)
                else:
                    pe.wait_ge(prod32_ready, prev.t)
                for s in range(BLOCK32):
                    for c in range(P // BLOCK32):
                        e = embT_v[prev.parity][:, BLOCK32 * c + s, :]
                        last = nc.tensor.matmul(gram[BLOCK32 * c:BLOCK32 * c + FEATURES, s, 0:FEATURES],
                                                e, e, start=True, stop=True)
                last.then_inc(gram_ready, 1)

            def transpose_extras(prev, n):
                if n <= 2:
                    pe.wait_ge(cleared, 5)
                pe.wait_ge(extra_ready, prev.t * 2 + 2)
                pe.wait_ge(dense_loaded[prev.parity], prev.half * 16 + 16)
                if n >= 2:
                    pe.wait_ge(h1T_ready, prev.t)
                for x in range(EXTRA_BLOCKS):
                    part = slice(x * P, (x + 1) * P)
                    last = nc.tensor.transpose(misc[:, part], extra[prev.parity][:, part], ident[:, :])
                last.then_inc(extra_transposed, 1)

            def multiply_extras(prev, n):
                if n == 1:
                    pe.wait_ge(w_lo_ready, W_PAIRS)
                pe.wait_ge(extra_lo_ready, prev.t + 1)
                for x in range(EXTRA_BLOCKS):
                    part = slice(x * P, (x + 1) * P)
                    last = three_passes(acc[prev.parity][:, :], extra_hi[:, part], extra_lo[:, part],
                                        FEATURES + x, False, x == EXTRA_BLOCKS - 1)
                last.then_inc(acc_ready, 1)

            def transpose_h1(prev, n):
                pe.wait_ge(h1_ready, prev.t + 1)
                for x in range(HIDDEN_BLOCKS):
                    part = slice(x * P, (x + 1) * P)
                    last = nc.tensor.transpose(misc[:, part], h1[:, part], ident[:, :])
                last.then_inc(h1_transposed, 1)

            def second_layer(prev, n):
                if n == 1:
                    pe.wait_ge(small_loaded, 48)
                else:
                    pe.wait_ge(h2_ready, prev.t)
                pe.wait_ge(h1T_ready, prev.t + 1)
                for x in range(HIDDEN_BLOCKS):
                    last = nc.tensor.matmul(second[:, :H2], h1T[:, x * P:(x + 1) * P], w2_sb[:, x, :],
                                            start=x == 0, stop=x == HIDDEN_BLOCKS - 1)
                last.then_inc(second_ready, 1)

            def step(tile, prev, n):
                if tile is not None:
                    transpose_rows(tile, 0, n)
                    transpose_rows(tile, 1, n)
                if prev is not None:
                    products(prev, n)
                later = {1: [transpose_extras], 2: [multiply_extras], 3: [transpose_h1], 4: [second_layer]}
                for q in range(NQ):
                    if tile is not None:
                        multiply_rows(tile, q, n)
                        if q + 2 < NQ:
                            transpose_rows(tile, q + 2, n)
                    if prev is not None:
                        for work in later.get(q, []):
                            work(prev, n)

            over_tiles(pe, step)


def kernel(**inputs):
    import concourse.bacc as bacc
    from concourse.bass_utils import run_bass_kernel_spmd

    w1 = np.asarray(inputs["W_top1"])
    bias_row = np.asarray(inputs["b_top1"])[None, :]
    dense_at = FEATURES * DIM + PAIRS
    w_extra = np.concatenate([w1[np.array(extra_rows())], w1[dense_at:dense_at + DENSE], bias_row,
                              np.zeros((EXTRAS - ONE_AT - 1, H1), w1.dtype)])
    arrays = {
        "ids": inputs["ids"],
        "dense": inputs["dense_ctx"],
        **{f"table{f}": inputs[f"tbl_{f}"] for f in range(FEATURES)},
        "w_embed": w1[:FEATURES * DIM].reshape(FEATURES, P, H1),
        "w_extra": w_extra.reshape(EXTRA_BLOCKS, P, H1),
        "w2": inputs["W_top2"],
        "b2": inputs["b_top2"],
        "w3": np.asarray(inputs["W_top3"]).reshape(H2),
    }
    arrays = {name: np.ascontiguousarray(a) for name, a in arrays.items()}

    nc = bacc.Bacc("TRN2", target_bir_lowering=False, num_devices=1)
    ap = {name: nc.dram_tensor(name, a.shape, mybir.dt.from_np(a.dtype), kind="ExternalInput").ap()
          for name, a in arrays.items()}
    out = nc.dram_tensor("out", (BATCH, 1), F32, kind="ExternalOutput").ap()
    build(nc, ap["ids"], ap["dense"], [ap[f"table{f}"] for f in range(FEATURES)], ap["w_embed"],
          ap["w_extra"], ap["w2"], ap["b2"], ap["w3"], out)
    r = run_bass_kernel_spmd(nc, [arrays], core_ids=[0])
    return r.results[0]["out"]
```

```python
from contextlib import ExitStack

import numpy as np

import concourse.bass as bass
from concourse import mybir

F32 = mybir.dt.float32
F32R = mybir.dt.float32r
I32 = mybir.dt.int32
ALU = mybir.AluOpType
ACT = mybir.ActivationFunctionType

P = 128
FEATURES = 27
DIM = 128
BATCH = 2048
DENSE = 16
H1 = 512
H2 = 256
TILES = BATCH // P
CHUNK = 4
CHUNKS = [list(range(max(f, 0), f + CHUNK)) for f in range(FEATURES % CHUNK - CHUNK, FEATURES, CHUNK)]
NQ = len(CHUNKS)

DIST = (FEATURES - 1) // 2
RUNS = FEATURES - 1
PAIRS = FEATURES * (FEATURES - 1) // 2
HALF = PAIRS - DIST * RUNS
DENSE_AT = PAIRS
ONE_AT = DENSE_AT + DENSE
EXTRA_BLOCKS = -(-(ONE_AT + 1) // P)
EXTRAS = EXTRA_BLOCKS * P
K_BLOCKS = FEATURES + EXTRA_BLOCKS
HIDDEN_BLOCKS = H1 // P
W2_BLOCKS = HIDDEN_BLOCKS * H2 // H1
W_PAIRS = (K_BLOCKS + W2_BLOCKS) // 2
W1_PAIRS = K_BLOCKS // 2
W_SLOTS = 3
BLOCK32 = 32


def extra_rows():
    flat = [(FEATURES + 1) * f + k for f in range(RUNS) for k in range(1, DIST + 1)]
    flat += [(FEATURES + 1) * f + DIST + 1 for f in range(HALF)]
    rows = []
    for v in flat:
        i, j = sorted(divmod(v, FEATURES))
        rows.append(FEATURES * DIM + i * FEATURES - i * (i + 1) // 2 + j - i - 1)
    assert sorted(rows) == list(range(FEATURES * DIM, FEATURES * DIM + PAIRS))
    return rows


class Tile:

    def __init__(self, t, half, parity):
        self.t, self.half, self.parity = t, half, parity

    def chunks(self, q):
        return self.t * NQ + (q + 1)

    def bank(self, q):
        return (self.parity * NQ + q) % 2


def tile_of(t):
    return Tile(t, t // 2, t % 2)


def over_tiles(engine, body):
    body(tile_of(0), None, 0)
    body(tile_of(1), tile_of(0), 1)
    with engine.Fori(1, TILES // 2) as i:
        even = Tile(i * 2, i, 0)
        odd = Tile(i * 2 + 1, i, 1)
        body(even, Tile(i * 2 - 1, i - 1, 1), 2)
        body(odd, even, 3)
    body(None, tile_of(TILES - 1), TILES)


def build(nc, ids, dense, tables, w_embed, w_extra, w2, b2, w3, out):
    with ExitStack() as ctx:
        def sb(name, shape, dt=F32):
            return ctx.enter_context(nc.sbuf_tensor(name, shape, dt))

        def pb(name):
            return ctx.enter_context(nc.psum_tensor(name, [P, 512], F32))

        def sem(name):
            return ctx.enter_context(nc.semaphore(name))

        w_hi = sb("w_hi", [P, K_BLOCKS + W2_BLOCKS, H1], F32R)
        w_lo = sb("w_lo", [P, K_BLOCKS + W2_BLOCKS, H1], F32R)
        w2_hi, w2_lo = (w[:, K_BLOCKS:, :].rearrange("p k (h n) -> p (k h) n", n=H2) for w in (w_hi, w_lo))
        b2_sb = sb("b2_sb", [P, H2])
        w3_sb = sb("w3_sb", [P, H2])
        ident = sb("ident", [P, P])
        ids_sb = [sb(f"ids{b}", [P, FEATURES], I32) for b in range(2)]
        rows = sb("rows", [P, FEATURES, DIM])
        embT = [sb(f"embT{b}", [P, P * FEATURES]) for b in range(2)]
        embT_v = [e[:, :].rearrange("d (s f) -> d s f", f=FEATURES) for e in embT]
        emb_hi = [sb(f"emb_hi{b}", [P, CHUNK * P], F32R) for b in range(2)]
        emb_lo = [sb(f"emb_lo{b}", [P, CHUNK * P], F32R) for b in range(2)]
        w_raw = embT[1][:, 0:W_SLOTS * 2 * H1].rearrange("p (s k n) -> p s k n", s=W_SLOTS, k=2)
        prod32 = sb("prod32", [P, FEATURES, BLOCK32])
        prod = sb("prod", [P, FEATURES * FEATURES])
        extra = [sb(f"extra{b}", [P, EXTRAS]) for b in range(2)]
        extra_hi = sb("extra_hi", [P, EXTRAS], F32R)
        extra_lo = sb("extra_lo", [P, EXTRAS], F32R)
        h1 = sb("h1", [P, H1])
        h1T_hi = sb("h1T_hi", [P, H1], F32R)
        h1T_lo = sb("h1T_lo", [P, H1], F32R)
        h2 = sb("h2", [P, H2])
        h2w = sb("h2w", [P, H2])
        y = [sb(f"y{b}", [P, 1]) for b in range(2)]

        acc = [pb(f"acc{b}") for b in range(2)]
        trans = [pb(f"trans{b}") for b in range(2)]
        gram = ctx.enter_context(nc.psum_tensor("gram", [P, BLOCK32, BLOCK32], F32))
        misc = pb("misc")
        second = pb("second")

        w_loaded = [sem(f"w_loaded{s}") for s in range(W_SLOTS)]
        small_loaded = sem("small_loaded")
        ids_loaded = [sem(f"ids_loaded{b}") for b in range(2)]
        dense_loaded = [sem(f"dense_loaded{b}") for b in range(2)]
        gathered = [sem(f"gathered{q}") for q in range(NQ)]
        stored = [sem(f"stored{b}") for b in range(2)]
        ident_zero = sem("ident_zero")
        ident_ready = sem("ident_ready")
        cleared = sem("cleared")
        w_hi_ready = sem("w_hi_ready")
        w_lo_ready = sem("w_lo_ready")
        rows_free = sem("rows_free")
        transposed = sem("transposed")
        hi_ready = sem("hi_ready")
        lo_ready = sem("lo_ready")
        raw_ready = sem("raw_ready")
        multiplied = sem("multiplied")
        gram_ready = sem("gram_ready")
        prod32_ready = sem("prod32_ready")
        prod_ready = sem("prod_ready")
        extra_ready = sem("extra_ready")
        extra_transposed = sem("extra_transposed")
        extra_hi_ready = sem("extra_hi_ready")
        extra_lo_ready = sem("extra_lo_ready")
        acc_ready = sem("acc_ready")
        h1_ready = sem("h1_ready")
        h1_transposed = sem("h1_transposed")
        h1T_hi_ready = sem("h1T_hi_ready")
        h1T_lo_ready = sem("h1T_lo_ready")
        second_ready = sem("second_ready")
        h2_ready = sem("h2_ready")
        y_ready = sem("y_ready")

        block = ctx.enter_context(nc.Block())

        @block.sync
        def _(sp):
            def load_ids(t, row, parity):
                sp.dma_start(ids_sb[parity][:, :], ids[row, :]).then_inc(ids_loaded[parity], 16)

            load_ids(0, bass.ds(0, P), 0)
            load_ids(1, bass.ds(P, P), 1)
            for j in range(W_PAIRS):
                if j >= W_SLOTS:
                    sp.wait_ge(w_lo_ready, j - W_SLOTS + 1)
                for half in range(2):
                    k = 2 * j + half
                    h = slice((k - K_BLOCKS) * P * (H1 // H2), (k - K_BLOCKS + 1) * P * (H1 // H2))
                    if k < FEATURES:
                        into, src = w_raw[:, j % W_SLOTS, half, :], w_embed[k]
                    elif k < K_BLOCKS:
                        into, src = w_raw[:, j % W_SLOTS, half, :], w_extra[k - FEATURES]
                    else:
                        into = w_raw[:, j % W_SLOTS, half, :].rearrange("p (h n) -> p h n", n=H2)
                        src = w2[h, :].rearrange("(h p) n -> p h n", p=P)
                    sp.dma_start(into, src).then_inc(w_loaded[j % W_SLOTS], 16)
            sp.dma_start(b2_sb[:, :], b2.partition_broadcast(P)).then_inc(small_loaded, 16)
            sp.dma_start(w3_sb[:, :], w3.partition_broadcast(P)).then_inc(small_loaded, 16)

            def step(tile, prev, n):
                if tile is not None:
                    if n >= 2:
                        sp.wait_ge(transposed, tile.t * NQ - NQ)
                        load_ids(tile.t, bass.ds(tile.t * P, P), tile.parity)
                        sp.wait_ge(extra_transposed, tile.t - 1)
                    else:
                        sp.wait_ge(cleared, 3)
                    sp.dma_start(extra[tile.parity][:, DENSE_AT:ONE_AT],
                                 dense[bass.ds(tile.t * P, P), :]).then_inc(dense_loaded[tile.parity], 16)
                if prev is not None and n >= 2:
                    store(Tile(prev.t - 1, prev.half if prev.parity else prev.half - 1, 1 - prev.parity))

            def store(done):
                sp.wait_ge(y_ready, done.t + 1)
                sp.dma_start(out[bass.ds(done.t * P, P), :], y[done.parity][:, :]).then_inc(
                    stored[done.parity], 16)

            over_tiles(sp, step)
            store(tile_of(TILES - 1))
            for b in range(2):
                sp.wait_ge(stored[b], 16 * (TILES // 2))

        @block.gpsimd
        def _(pool):
            nc.gpsimd.memset(ident[:, :], 0.0).then_inc(ident_zero, 1)
            pool.wait_ge(ident_zero, 1)
            nc.gpsimd.affine_select(out=ident[:, :], in_=ident[:, :], compare_op=ALU.not_equal, fill=1.0,
                                    base=0, pattern=[[-1, P]], channel_multiplier=1).then_inc(ident_ready, 1)

            def step(tile, prev, n):
                if tile is None:
                    return
                pool.wait_ge(ids_loaded[tile.parity], tile.half * 16 + 16)
                for q, features in enumerate(CHUNKS):
                    if n >= 1:
                        pool.wait_ge(transposed, tile.chunks(q) - NQ)
                    pool.sem_inc(rows_free, 1)
                    for f in features:
                        nc.gpsimd.indirect_dma_start(
                            rows[:, f, :], None, tables[f],
                            bass.IndirectOffsetOnAxis(ap=ids_sb[tile.parity][:, f:f + 1], axis=0),
                        ).then_inc(gathered[q], 16)

            over_tiles(pool, step)

        @block.scalar
        def _(act):
            def split_weights(j):
                act.wait_ge(w_loaded[j % W_SLOTS], 32 * (j // W_SLOTS + 1))
                nc.scalar.copy(w_hi[:, 2 * j:2 * j + 2, :], w_raw[:, j % W_SLOTS]).then_inc(w_hi_ready, 1)

            def embedding_hi(tile, q, n):
                width = len(CHUNKS[q]) * P
                b = tile.bank(q)
                act.wait_ge(transposed, tile.chunks(q))
                if n >= 1 or q >= 2:
                    act.wait_ge(multiplied, tile.chunks(q) - 2)
                nc.scalar.copy(emb_hi[b][:, :width], trans[b][:, :width]).then_inc(hi_ready, 1)

            def compact_products(prev, n):
                act.wait_ge(prod32_ready, prev.t + 1)
                if n >= 2:
                    act.wait_ge(extra_ready, prev.t * 2)
                nc.scalar.copy(prod[:, :].rearrange("p (g f) -> p g f", f=FEATURES),
                               prod32[:, :, 0:FEATURES]).then_inc(prod_ready, 1)

            def extras_hi(prev, n):
                act.wait_ge(extra_transposed, prev.t + 1)
                if n >= 2:
                    act.wait_ge(acc_ready, prev.t)
                nc.scalar.copy(extra_hi[:, :], misc[:, :EXTRAS]).then_inc(extra_hi_ready, 1)

            def relu1(prev, n):
                act.wait_ge(acc_ready, prev.t + 1)
                if n >= 2:
                    act.wait_ge(h1_transposed, prev.t)
                nc.scalar.activation(h1[:, :], acc[prev.parity][:, :], ACT.Relu).then_inc(h1_ready, 1)

            def h1_hi(prev, n):
                act.wait_ge(h1_transposed, prev.t + 1)
                if n >= 2:
                    act.wait_ge(second_ready, prev.t)
                nc.scalar.copy(h1T_hi[:, :], misc[:, :]).then_inc(h1T_hi_ready, 1)

            def step(tile, prev, n):
                before = {1: compact_products, 2: extras_hi, 3: relu1, 4: h1_hi}
                for q in range(NQ):
                    if n == 0:
                        split_weights(2 * q)
                        split_weights(2 * q + 1)
                    if prev is not None and q in before:
                        before[q](prev, n)
                    if tile is not None:
                        embedding_hi(tile, q, n)
                if n == 0:
                    for j in range(2 * NQ, W_PAIRS):
                        split_weights(j)

            over_tiles(act, step)

        @block.vector
        def _(dve):
            nc.vector.memset(gram[:, :, :], 0.0).then_inc(cleared, 1)
            for b in range(2):
                nc.vector.memset(extra[b][:, ONE_AT:], 0.0).then_inc(cleared, 1)
            dve.wait_ge(cleared, 3)
            for b in range(2):
                nc.vector.memset(extra[b][:, ONE_AT:ONE_AT + 1], 1.0).then_inc(cleared, 1)

            def split_weights(j):
                dve.wait_ge(w_hi_ready, j + 1)
                nc.vector.tensor_tensor(w_lo[:, 2 * j:2 * j + 2, :], w_raw[:, j % W_SLOTS],
                                        w_hi[:, 2 * j:2 * j + 2, :].bitcast(F32), ALU.subtract).then_inc(w_lo_ready, 1)

            def embedding_lo(tile, q, n):
                count = len(CHUNKS[q])
                b = tile.bank(q)
                dve.wait_ge(hi_ready, tile.chunks(q))
                nc.vector.tensor_tensor(emb_lo[b][:, :count * P], trans[b][:, :count * P],
                                        emb_hi[b][:, :count * P].bitcast(F32), ALU.subtract).then_inc(lo_ready, 1)
                if q == 0 and n == 1:
                    dve.wait_ge(w_lo_ready, W_PAIRS)
                if q == 0 and n >= 2:
                    dve.wait_ge(gram_ready, tile.t - 1)
                f0 = CHUNKS[q][0]
                nc.vector.tensor_copy(
                    embT_v[tile.parity][:, :, f0:f0 + count],
                    trans[b][:, :count * P].rearrange("d (f s) -> d s f", f=count)).then_inc(raw_ready, 1)

            def products_by_sample(prev, n):
                dve.wait_ge(gram_ready, prev.t + 1)
                if n >= 2:
                    dve.wait_ge(prod_ready, prev.t)
                nc.vector.transpose(prod32[:, :, :],
                                    gram[:, :, 0:FEATURES].rearrange("p s g -> p g s")).then_inc(prod32_ready, 1)

            def extras(prev, n):
                dve.wait_ge(prod_ready, prev.t + 1)
                if n >= 3:
                    dve.wait_ge(extra_transposed, prev.t - 1)
                runs = prod[:, 0:RUNS * (FEATURES + 1)].rearrange("p (f k) -> p f k", k=FEATURES + 1)
                nc.vector.tensor_copy(extra[prev.parity][:, 0:RUNS * DIST].rearrange("p (f k) -> p f k", k=DIST),
                                      runs[:, :, 1:DIST + 1]).then_inc(extra_ready, 1)
                nc.vector.tensor_copy(extra[prev.parity][:, RUNS * DIST:PAIRS],
                                      runs[:, 0:HALF, DIST + 1]).then_inc(extra_ready, 1)

            def extras_lo(prev, n):
                dve.wait_ge(extra_hi_ready, prev.t + 1)
                nc.vector.tensor_tensor(extra_lo[:, :], misc[:, :EXTRAS], extra_hi[:, :].bitcast(F32),
                                        ALU.subtract).then_inc(extra_lo_ready, 1)

            def h1_lo(prev, n):
                dve.wait_ge(h1T_hi_ready, prev.t + 1)
                nc.vector.tensor_tensor(h1T_lo[:, :], misc[:, :], h1T_hi[:, :].bitcast(F32),
                                        ALU.subtract).then_inc(h1T_lo_ready, 1)

            def last_layers(prev, n):
                if n == 1:
                    dve.wait_ge(small_loaded, 32)
                dve.wait_ge(second_ready, prev.t + 1)
                if n >= 2:
                    dve.wait_ge(y_ready, prev.t)
                nc.vector.tensor_tensor(h2[:, :], second[:, :H2], b2_sb[:, :], ALU.add).then_inc(h2_ready, 1)
                dve.wait_ge(h2_ready, prev.t + 1)
                if n >= 3:
                    dve.wait_ge(stored[prev.parity], prev.half * 16)
                nc.vector.scalar_tensor_tensor(out=h2w[:, :], in0=h2[:, :], scalar=0.0, in1=w3_sb[:, :],
                                               op0=ALU.max, op1=ALU.mult,
                                               accum_out=y[prev.parity][:, :]).then_inc(y_ready, 1)

            def step(tile, prev, n):
                before = {1: [products_by_sample, extras], 2: [extras_lo], 4: [h1_lo], 5: [last_layers]}
                for q in range(NQ):
                    if n == 0:
                        split_weights(2 * q)
                        split_weights(2 * q + 1)
                    if prev is not None:
                        for work in before.get(q, []):
                            work(prev, n)
                    if tile is not None:
                        embedding_lo(tile, q, n)
                if n == 0:
                    for j in range(2 * NQ, W_PAIRS):
                        split_weights(j)

            over_tiles(dve, step)

        @block.tensor
        def _(pe):
            pe.wait_ge(ident_ready, 1)

            def transpose_rows(tile, q, n):
                pe.wait_ge(gathered[q], tile.t * (16 * len(CHUNKS[q])) + 16 * len(CHUNKS[q]))
                if n >= 1 or q >= 2:
                    pe.wait_ge(raw_ready, tile.chunks(q) - 2)
                for a, f in enumerate(CHUNKS[q]):
                    last = nc.tensor.transpose(trans[tile.bank(q)][:, a * P:(a + 1) * P], rows[:, f, :], ident[:, :])
                last.then_inc(transposed, 1)

            def three_passes(into, hi, lo, weight_hi, weight_lo, first, final):
                nc.tensor.matmul(into, hi, weight_hi, start=first, stop=False)
                nc.tensor.matmul(into, hi, weight_lo, start=False, stop=False)
                return nc.tensor.matmul(into, lo, weight_hi, start=False, stop=final)

            def multiply_rows(tile, q, n):
                if n == 0:
                    pe.wait_ge(w_lo_ready, 2 * q + 2)
                if q == 0 and n >= 2:
                    pe.wait_ge(h1_ready, tile.t - 1)
                pe.wait_ge(lo_ready, tile.chunks(q))
                for a, f in enumerate(CHUNKS[q]):
                    part = slice(a * P, (a + 1) * P)
                    last = three_passes(acc[tile.parity][:, :], emb_hi[tile.bank(q)][:, part],
                                        emb_lo[tile.bank(q)][:, part], w_hi[:, f, :], w_lo[:, f, :],
                                        f == 0, False)
                last.then_inc(multiplied, 1)

            def products(prev, n):
                pe.wait_ge(raw_ready, prev.t * NQ + NQ)
                if n == 1:
                    pe.wait_ge(cleared, 1)
                else:
                    pe.wait_ge(prod32_ready, prev.t)
                for s in range(BLOCK32):
                    for c in range(P // BLOCK32):
                        e = embT_v[prev.parity][:, BLOCK32 * c + s, :]
                        last = nc.tensor.matmul(gram[BLOCK32 * c:BLOCK32 * c + FEATURES, s, 0:FEATURES],
                                                e, e, start=True, stop=True)
                last.then_inc(gram_ready, 1)

            def transpose_extras(prev, n):
                if n <= 2:
                    pe.wait_ge(cleared, 5)
                pe.wait_ge(extra_ready, prev.t * 2 + 2)
                pe.wait_ge(dense_loaded[prev.parity], prev.half * 16 + 16)
                if n >= 2:
                    pe.wait_ge(h1T_lo_ready, prev.t)
                for x in range(EXTRA_BLOCKS):
                    part = slice(x * P, (x + 1) * P)
                    last = nc.tensor.transpose(misc[:, part], extra[prev.parity][:, part], ident[:, :])
                last.then_inc(extra_transposed, 1)

            def multiply_extras(prev, n):
                if n == 1:
                    pe.wait_ge(w_lo_ready, W1_PAIRS)
                pe.wait_ge(extra_lo_ready, prev.t + 1)
                for x in range(EXTRA_BLOCKS):
                    part = slice(x * P, (x + 1) * P)
                    last = three_passes(acc[prev.parity][:, :], extra_hi[:, part], extra_lo[:, part],
                                        w_hi[:, FEATURES + x, :], w_lo[:, FEATURES + x, :], False, x == EXTRA_BLOCKS - 1)
                last.then_inc(acc_ready, 1)

            def transpose_h1(prev, n):
                pe.wait_ge(h1_ready, prev.t + 1)
                for x in range(HIDDEN_BLOCKS):
                    part = slice(x * P, (x + 1) * P)
                    last = nc.tensor.transpose(misc[:, part], h1[:, part], ident[:, :])
                last.then_inc(h1_transposed, 1)

            def second_layer(prev, n):
                if n == 1:
                    pe.wait_ge(w_lo_ready, W_PAIRS)
                else:
                    pe.wait_ge(h2_ready, prev.t)
                pe.wait_ge(h1T_lo_ready, prev.t + 1)
                for x in range(HIDDEN_BLOCKS):
                    part = slice(x * P, (x + 1) * P)
                    last = three_passes(second[:, :H2], h1T_hi[:, part], h1T_lo[:, part],
                                        w2_hi[:, x, :], w2_lo[:, x, :], x == 0, x == HIDDEN_BLOCKS - 1)
                last.then_inc(second_ready, 1)

            def step(tile, prev, n):
                if tile is not None and n != 1:
                    transpose_rows(tile, 0, n)
                if prev is not None:
                    products(prev, n)
                    if n == 1:
                        transpose_rows(tile, 0, n)
                    multiply_rows(prev, NQ - 1, n - 1)
                if tile is not None:
                    transpose_rows(tile, 1, n)
                after = {0: transpose_extras, 1: multiply_extras, 2: transpose_h1, 3: second_layer}
                for q in range(NQ - 1):
                    if tile is not None:
                        multiply_rows(tile, q, n)
                    if prev is not None and q in after:
                        after[q](prev, n)
                    if tile is not None and q + 2 < NQ:
                        transpose_rows(tile, q + 2, n)

            over_tiles(pe, step)


def kernel(**inputs):
    import concourse.bacc as bacc
    from concourse.bass_utils import run_bass_kernel_spmd

    w1 = np.asarray(inputs["W_top1"])
    bias_row = np.asarray(inputs["b_top1"])[None, :]
    dense_at = FEATURES * DIM + PAIRS
    w_extra = np.concatenate([w1[np.array(extra_rows())], w1[dense_at:dense_at + DENSE], bias_row,
                              np.zeros((EXTRAS - ONE_AT - 1, H1), w1.dtype)])
    arrays = {
        "ids": inputs["ids"],
        "dense": inputs["dense_ctx"],
        **{f"table{f}": inputs[f"tbl_{f}"] for f in range(FEATURES)},
        "w_embed": w1[:FEATURES * DIM].reshape(FEATURES, P, H1),
        "w_extra": w_extra.reshape(EXTRA_BLOCKS, P, H1),
        "w2": inputs["W_top2"],
        "b2": inputs["b_top2"],
        "w3": np.asarray(inputs["W_top3"]).reshape(H2),
    }
    arrays = {name: np.ascontiguousarray(a) for name, a in arrays.items()}

    nc = bacc.Bacc("TRN2", target_bir_lowering=False, num_devices=1)
    ap = {name: nc.dram_tensor(name, a.shape, mybir.dt.from_np(a.dtype), kind="ExternalInput").ap()
          for name, a in arrays.items()}
    out = nc.dram_tensor("out", (BATCH, 1), F32, kind="ExternalOutput").ap()
    build(nc, ap["ids"], ap["dense"], [ap[f"table{f}"] for f in range(FEATURES)], ap["w_embed"],
          ap["w_extra"], ap["w2"], ap["b2"], ap["w3"], out)
    r = run_bass_kernel_spmd(nc, [arrays], core_ids=[0])
    return r.results[0]["out"]
```
